# Optimizing a Trainium2 kernel written in Bass

```python
import numpy as np
import jax
import jax.numpy as jnp

def _softmax(x, axis=-1):
    return jax.nn.softmax(x, axis=axis)

def _gelu(x):
    return jax.nn.gelu(x, approximate=True)

def _silu(x):
    return jax.nn.silu(x)

def _sigmoid(x):
    return jax.nn.sigmoid(x)

def _layernorm(x, axis=-1, eps=1e-05):
    m = jnp.mean(x, axis=axis, keepdims=True)
    v = jnp.var(x, axis=axis, keepdims=True)
    return (x - m) / jnp.sqrt(v + eps)

def _scatter_add(tgt, idx, src, axis=0):
    return tgt.at[idx].add(src)

def _segment_sum(src, seg, n):
    return jax.ops.segment_sum(src, seg, n)
kernel_name = 'mk_prb_d1_jaxref_r8_7cb9b8'

def setup_inputs(seed: int=0):
    np.random.seed(seed)
    _w = jnp.asarray

    def _L0_attn_setup():
        import jax, jax.numpy as jnp
        import numpy as np
        DIM = 128
        KV_DIM = 128
        WINDOW_SIZE = 64
        B, S = (2, 256)

        def _sliding_window_attention(m, q_w, q_b, k_w, k_b, v_w, v_b, window_size):
            Bsz, Seq, D = m.shape
            q = m @ q_w + q_b
            k = m @ k_w + k_b
            v = m @ v_w + v_b
            half = window_size // 2
            offsets = jnp.arange(-half, half + 1)
            idx = jnp.arange(Seq)[:, None] + offsets[None, :]
            valid = (idx >= 0) & (idx < Seq)
            idx_c = jnp.clip(idx, 0, Seq - 1)
            k_band = k[:, idx_c]
            v_band = v[:, idx_c]
            scale = 1.0 / jnp.sqrt(jnp.float32(D))
            scores = jnp.einsum('bsd,bswd->bsw', q, k_band) * scale
            scores = jnp.where(valid[None, :, :], scores, -jnp.inf)
            weights = jax.nn.softmax(scores, axis=-1)
            return jnp.einsum('bsw,bswd->bsd', weights, v_band)
        key = jax.random.key(seed)
        ks = jax.random.split(key, 12)
        w_scale = 1.0 / np.sqrt(DIM)
        return {'x': jax.random.normal(ks[0], (B, S, DIM), dtype=jnp.float32), 'nm_w1': jax.random.normal(ks[1], (DIM, KV_DIM), dtype=jnp.float32) * w_scale, 'nm_b1': jnp.zeros((KV_DIM,), dtype=jnp.float32), 'nm_w2': jax.random.normal(ks[2], (KV_DIM, DIM), dtype=jnp.float32) * w_scale, 'nm_b2': jnp.zeros((DIM,), dtype=jnp.float32), 'q_w': jax.random.normal(ks[3], (DIM, DIM), dtype=jnp.float32) * w_scale, 'q_b': jnp.zeros((DIM,), dtype=jnp.float32), 'k_w': jax.random.normal(ks[4], (DIM, DIM), dtype=jnp.float32) * w_scale, 'k_b': jnp.zeros((DIM,), dtype=jnp.float32), 'v_w': jax.random.normal(ks[5], (DIM, DIM), dtype=jnp.float32) * w_scale, 'v_b': jnp.zeros((DIM,), dtype=jnp.float32)}
    _L0_attn_in = _L0_attn_setup()

    def _L0_ffn_setup():
        import jax, jax.numpy as jnp
        import numpy as np
        B, S, D = (2, 64, 128)
        E, K, I = (16, 8, 128)
        I_SH = 128
        ROUTE_SCALE = 2.826
        key = jax.random.key(seed)
        ks = jax.random.split(key, 8)
        s = 0.02
        return {'x': jax.random.normal(ks[0], (B, S, D), dtype=jnp.float32), 'gate_w': jax.random.normal(ks[1], (E, D), dtype=jnp.float32) * s, 'expert_bias': jnp.zeros((E,), dtype=jnp.float32), 'w_gate': jax.random.normal(ks[2], (E, I, D), dtype=jnp.float32) * s, 'w_up': jax.random.normal(ks[3], (E, I, D), dtype=jnp.float32) * s, 'w_down': jax.random.normal(ks[4], (E, D, I), dtype=jnp.float32) * s, 'shared_gate_w': jax.random.normal(ks[5], (I_SH, D), dtype=jnp.float32) * s, 'shared_up_w': jax.random.normal(ks[6], (I_SH, D), dtype=jnp.float32) * s, 'shared_down_w': jax.random.normal(ks[7], (D, I_SH), dtype=jnp.float32) * s}
    _L0_ffn_in = _L0_ffn_setup()
    _d = {'L0_attn_x': _L0_attn_in['x'], 'L0_attn_nm_w1': _L0_attn_in['nm_w1'], 'L0_attn_nm_b1': _L0_attn_in['nm_b1'], 'L0_attn_nm_w2': _L0_attn_in['nm_w2'], 'L0_attn_nm_b2': _L0_attn_in['nm_b2'], 'L0_attn_q_w': _L0_attn_in['q_w'], 'L0_attn_q_b': _L0_attn_in['q_b'], 'L0_attn_k_w': _L0_attn_in['k_w'], 'L0_attn_k_b': _L0_attn_in['k_b'], 'L0_attn_v_w': _L0_attn_in['v_w'], 'L0_attn_v_b': _L0_attn_in['v_b'], 'L0_ffn_gate_w': _L0_ffn_in['gate_w'], 'L0_ffn_expert_bias': _L0_ffn_in['expert_bias'], 'L0_ffn_w_gate': _L0_ffn_in['w_gate'], 'L0_ffn_w_up': _L0_ffn_in['w_up'], 'L0_ffn_w_down': _L0_ffn_in['w_down'], 'L0_ffn_shared_gate_w': _L0_ffn_in['shared_gate_w'], 'L0_ffn_shared_up_w': _L0_ffn_in['shared_up_w'], 'L0_ffn_shared_down_w': _L0_ffn_in['shared_down_w']}
    _x0 = _d['L0_attn_x']
    _d['L0_attn_x'] = jax.random.normal(jax.random.fold_in(jax.random.key(seed), 1), (32, 256, 128), dtype=_x0.dtype)
    del _x0
    return _d

def reference(L0_attn_x, L0_attn_nm_w1, L0_attn_nm_b1, L0_attn_nm_w2, L0_attn_nm_b2, L0_attn_q_w, L0_attn_q_b, L0_attn_k_w, L0_attn_k_b, L0_attn_v_w, L0_attn_v_b, L0_ffn_gate_w, L0_ffn_expert_bias, L0_ffn_w_gate, L0_ffn_w_up, L0_ffn_w_down, L0_ffn_shared_gate_w, L0_ffn_shared_up_w, L0_ffn_shared_down_w):

    def _L0_attn_ref(x, nm_w1, nm_b1, nm_w2, nm_b2, q_w, q_b, k_w, k_b, v_w, v_b):
        import jax, jax.numpy as jnp
        import numpy as np
        DIM = 128
        KV_DIM = 128
        WINDOW_SIZE = 64
        B, S = (2, 256)

        def _sliding_window_attention(m, q_w, q_b, k_w, k_b, v_w, v_b, window_size):
            Bsz, Seq, D = m.shape
            q = m @ q_w + q_b
            k = m @ k_w + k_b
            v = m @ v_w + v_b
            half = window_size // 2
            offsets = jnp.arange(-half, half + 1)
            idx = jnp.arange(Seq)[:, None] + offsets[None, :]
            valid = (idx >= 0) & (idx < Seq)
            idx_c = jnp.clip(idx, 0, Seq - 1)
            k_band = k[:, idx_c]
            v_band = v[:, idx_c]
            scale = 1.0 / jnp.sqrt(jnp.float32(D))
            scores = jnp.einsum('bsd,bswd->bsw', q, k_band) * scale
            scores = jnp.where(valid[None, :, :], scores, -jnp.inf)
            weights = jax.nn.softmax(scores, axis=-1)
            return jnp.einsum('bsw,bswd->bsd', weights, v_band)
        h = jax.nn.relu(x @ nm_w1 + nm_b1)
        m = h @ nm_w2 + nm_b2
        return _sliding_window_attention(m, q_w, q_b, k_w, k_b, v_w, v_b, WINDOW_SIZE)

    def _L0_ffn_ref(x, gate_w, expert_bias, w_gate, w_up, w_down, shared_gate_w, shared_up_w, shared_down_w):
        import jax, jax.numpy as jnp
        import numpy as np
        B, S, D = (2, 64, 128)
        E, K, I = (16, 8, 128)
        I_SH = 128
        ROUTE_SCALE = 2.826
        gates = jnp.einsum('bsd,ed->bse', x, gate_w)
        scores = jax.nn.sigmoid(gates.astype(jnp.float32))
        sel_scores = scores + expert_bias
        _, inds = jax.lax.top_k(sel_scores, K)
        selected = jnp.take_along_axis(scores, inds, axis=-1)
        selected = selected / selected.sum(axis=-1, keepdims=True)
        selected = selected * ROUTE_SCALE
        onehot = jax.nn.one_hot(inds, E, dtype=selected.dtype)
        combine = jnp.einsum('bske,bsk->bse', onehot, selected)
        hg = jnp.einsum('bsd,eid->bsei', x, w_gate)
        hu = jnp.einsum('bsd,eid->bsei', x, w_up)
        h = jax.nn.silu(hg) * hu
        ye = jnp.einsum('bsei,edi->bsed', h, w_down)
        y = jnp.einsum('bsed,bse->bsd', ye, combine).astype(x.dtype)
        g = jnp.einsum('bsd,id->bsi', x, shared_gate_w)
        u = jnp.einsum('bsd,id->bsi', x, shared_up_w)
        y = y + jnp.einsum('bsi,di->bsd', jax.nn.silu(g) * u, shared_down_w)
        return y
    x = L0_attn_x
    xn = _layernorm(x, axis=-1)
    x = x + _L0_attn_ref(xn, L0_attn_nm_w1, L0_attn_nm_b1, L0_attn_nm_w2, L0_attn_nm_b2, L0_attn_q_w, L0_attn_q_b, L0_attn_k_w, L0_attn_k_b, L0_attn_v_w, L0_attn_v_b) + _L0_ffn_ref(xn, L0_ffn_gate_w, L0_ffn_expert_bias, L0_ffn_w_gate, L0_ffn_w_up, L0_ffn_w_down, L0_ffn_shared_gate_w, L0_ffn_shared_up_w, L0_ffn_shared_down_w)
    return x

_drawn_inputs = setup_inputs


def setup_inputs(seed=0):
    import zlib

    import numpy as np

    out = dict(_drawn_inputs(seed))
    spreads = {'L0_attn_nm_b1': (0.0, 0.8),
     'L0_attn_nm_b2': (0.0, 0.46),
     'L0_attn_q_b': (0.0, 2.0),
     'L0_attn_k_b': (0.0, 2.0),
     'L0_attn_v_b': (0.0, 0.501),
     'L0_ffn_expert_bias': (0.0, 0.8)}
    factors = {'L0_ffn_gate_w': 8.0,
     'L0_ffn_w_gate': 8.0,
     'L0_ffn_w_up': 8.0,
     'L0_ffn_w_down': 8.0,
     'L0_ffn_shared_gate_w': 8.0,
     'L0_ffn_shared_up_w': 8.0,
     'L0_ffn_shared_down_w': 8.0,
     'L0_attn_nm_w1': 3.331,
     'L0_attn_q_w': 7.263,
     'L0_attn_k_w': 5.544}
    for name, (base, spread) in spreads.items():
        noise = np.random.default_rng([zlib.crc32(name.encode()), seed]).standard_normal(out[name].shape)
        drawn = base * np.exp(spread * noise) if base else spread * noise
        out[name] = jnp.asarray(drawn.astype(out[name].dtype))
    for name, factor in factors.items():
        out[name] = (out[name] * factor).astype(out[name].dtype)
    return out
```

```python
from contextlib import ExitStack

import concourse.bass as bass
from concourse import mybir

F32 = mybir.dt.float32
F32R = mybir.dt.float32r
BF16 = mybir.dt.bfloat16
F16 = mybir.dt.float16
ALU = mybir.AluOpType
ACT = mybir.ActivationFunctionType
AX = mybir.AxisListType

P = 128
SEQ = 256
SEQS = 32
T = 512
TILES = T // P
NB = T // SEQ
GROUPS = SEQS * SEQ // T
E = 16
TOPK = 8
STEPS = E + 1
HALF = 32
WIN = P + HALF
EPS = 1e-5
ROUTE_SCALE = 2.826
SCALE = float(P) ** -0.5
MASKED = -1e30
TAKEN = -3e38
CHUNK = 4
NCHUNK = E // CHUNK
PAIRS3 = [(0, 0), (0, 1), (1, 0)]
PAIRS6 = [(0, 0), (0, 1), (1, 0), (1, 1), (0, 2), (2, 0)]
PAIRSPV = [(0, 0), (0, 1), (1, 0), (1, 1), (2, 0)]


def layer(nc, x, x_t, w1, b1, w2, b2, qw, qb, kw, kb, vw, vb, gate_w, expert_bias,
          wexp, out_t, c_dram):
    ctx = ExitStack()
    with ctx:
        def sb(name, shape, dt=F32):
            return ctx.enter_context(nc.sbuf_tensor(name, shape, dt))

        def pb(name):
            return ctx.enter_context(nc.psum_tensor(name, [P, T], F32))

        def sem(name):
            return ctx.enter_context(nc.semaphore(name))

        NA = 6
        att_raw = sb("att_raw", [P, NA, P])
        att_w = [sb("att_w_hi", [P, NA, P], F32R), sb("att_w_lo", [P, NA, P], F32R)]
        exp_raw = sb("exp_raw", [P, STEPS, 3 * P])
        exp_w = [sb("exp_w_hi", [P, STEPS, 3 * P], F32R), sb("exp_w_lo", [P, STEPS, 3 * P], F32R)]
        bias = sb("bias", [P, 5])
        ebias = sb("ebias", [P, TILES, E])
        ident = sb("ident", [P, P])
        ident_b = sb("ident_b", [P, P], BF16)
        mask = sb("mask", [P, 2, WIN], BF16)
        power = sb("power", [P, TILES])
        xin = [sb(f"xin{i}", [P, TILES, P]) for i in range(2)]
        xres = [sb(f"xres{i}", [P, T]) for i in range(2)]
        stats = sb("stats", [P, TILES, 6])
        mv = sb("mv", [P, TILES, 2])
        var_eps = sb("var_eps", [P, TILES])
        rstd = sb("rstd", [P, TILES])
        xn = sb("xn", [P, TILES, P])
        xn_t = [[sb(f"xn_hi{i}", [P, T], F32R), sb(f"xn_lo{i}", [P, T], F32R)] for i in range(2)]
        hid = sb("hid", [P, T])
        hid_t = [sb("hid_hi", [P, T], F32R), sb("hid_lo", [P, T], F32R)]
        m_t = [sb("m_hi", [P, T], F32R), sb("m_lo", [P, T], F32R)]
        q_rest = sb("q_rest", [P, T])
        k_rest = sb("k_rest", [P, T])
        v_rest = sb("v_rest", [P, T])
        q_t = [sb(f"q_t{i}", [P, T], BF16) for i in range(3)]
        k_t = [sb(f"k_t{i}", [P, T], BF16) for i in range(3)]
        v_t = sb("v_t", [P, T])
        v_nat = [sb(f"v_nat{i}", [P, TILES, P], BF16) for i in range(3)]
        neg_max = sb("neg_max", [P, TILES])
        exp_bias = sb("exp_bias", [P, TILES])
        row_sum = sb("row_sum", [P, TILES])
        row_inv = sb("row_inv", [P, TILES])
        prob = sb("prob", [P, TILES, SEQ])
        prob_n = sb("prob_n", [P, TILES, SEQ])
        p_t = [sb("p_hi", [P, NB, 2, WIN], F16), sb("p_lo", [P, NB, 2, WIN], F16)]
        gate_e = sb("gate_e", [P, T])
        gate_1 = sb("gate_1", [P, TILES, E])
        score = sb("score", [P, TILES, E])
        select = sb("select", [P, TILES, E])
        top8 = sb("top8", [P, TILES, TOPK])
        rest = sb("rest", [P, TILES, E])
        chosen = sb("chosen", [P, TILES, E])
        weight = sb("weight", [P, TILES, E])
        wsum = sb("wsum", [P, TILES])
        winv = sb("winv", [P, TILES])
        comb = sb("comb", [P, TILES, P])
        comb_t = sb("comb_t", [E, T])
        comb_b = sb("comb_b", [P, E, T])
        silu = [sb(f"silu{i}", [P, T]) for i in range(2)]
        silu_c = [sb(f"silu_c{i}", [P, T]) for i in range(2)]
        h = [sb(f"h{i}", [P, T]) for i in range(2)]
        h_t = [[sb(f"h_hi{i}", [P, T], F32R), sb(f"h_lo{i}", [P, T], F32R)] for i in range(2)]
        y_sb = [sb(f"y_sb{i}", [P, T]) for i in range(2)]
        ps_g = [pb(f"ps_g{i}") for i in range(2)]
        ps_u = [pb(f"ps_u{i}") for i in range(2)]
        ps_y = pb("ps_y")
        bank = [pb(f"bank{i}") for i in range(3)]

        s_attw_in = sem("attw_loaded")
        s_expw_in = [sem(f"expw_loaded{i}") for i in range(4)]
        s_small_in = sem("small_loaded")
        s_pad = sem("gate_pad_cleared")
        s_const0 = sem("const_cleared")
        s_const1 = sem("const_band_low")
        s_const = sem("const_ready")
        s_dve_const = sem("dve_const_ready")
        s_attw_hi = sem("attw_hi_ready")
        s_attw = sem("attw_ready")
        s_expw_hi = sem("expw_hi_ready")
        s_expw = sem("expw_ready")
        s_xin = [sem(f"x_loaded{i}") for i in range(2)]
        s_xres = [sem(f"xres_loaded{i}") for i in range(2)]
        s_g = sem("gate_prod_ready")
        s_u = sem("up_prod_ready")
        s_silu = sem("silu_ready")
        s_silu_c = sem("silu_c_ready")
        s_h = sem("h_ready")
        s_h_hi = sem("h_hi_ready")
        s_h_lo = sem("h_lo_ready")
        s_down = sem("down_done")
        s_y_out = sem("y_evacuated")
        s_stored = [sem(f"y_stored{i}") for i in range(2)]
        s_pv = sem("pv_done")
        s_held = sem("held")
        names = """bn aggr var_eps rstd xn xn_tp xn_hi xn_lo
            hid_mm hid hid_hi hid_lo m_mm m_hi m_lo q_mm q0 q_rest q1 q2 k_mm k0 k_rest k1 k2
            vt_mm vt v_tp v0 v_rest v1 v2 sc0_mm sc1_mm nmax0 nmax1 ebias0 ebias1 gate_mm
            exp0 exp1 inv0 inv1 pn0 pn1 gate_e gate_tp gate_1 score select top8 rest
            chosen weight wsum winv comb comb_tp comb_t pt0_tp pt1_tp
            p0_hi p0_lo p1_hi p1_lo""".split()
        S = {n: sem(n) for n in names}
        s_comb_st = sem("comb_stored")
        s_comb_b = [sem(f"comb_b_loaded{i}") for i in range(NCHUNK)]

        block = ctx.enter_context(nc.Block())

        def program(eng, prepare, expert, stage, finish):
            for s in range(STEPS):
                prepare(s)
                stage(0, 0, s, True)
            for s in range(STEPS):
                expert(0, 0, s, True)
                stage(1, 1, s, False)
            with eng.Fori(0, (GROUPS - 2) // 2) as pair:
                for k in (1, 2):
                    g = pair * 2 + k
                    for s in range(STEPS):
                        expert(g, k % 2, s, False)
                        stage(g + 1, (k + 1) % 2, s, False)
            for s in range(STEPS):
                expert(GROUPS - 1, (GROUPS - 1) % 2, s, False)
            finish()

        def hold(eng):
            eng.sem_inc(s_held, 1)

        def early(g):
            return isinstance(g, int) and g < 2

        def last_group(g):
            return isinstance(g, int) and g == GROUPS - 1

        def nothing(*a):
            pass

        def in_band(b):
            return b[:].rearrange("p (k c) -> p k c", k=2)[:, :, 0:WIN]

        @block.sync
        def _(sp):
            def load_x(g, par):
                if not early(g):
                    sp.wait_ge(S["xn"], g - 1)
                    hold(sp)
                sp.dma_start(xin[par][:], x[bass.ds(g * T, T), :].rearrange("(a p) d -> p a d", p=P))\
                    .then_inc(s_xin[par], 16)

            def load_res(g, par):
                if not early(g):
                    sp.wait_ge(s_y_out, g - 1)
                    hold(sp)
                sp.dma_start(xres[par][:], x_t[:, bass.ds(g * T, T)]).then_inc(s_xres[par], 16)

            def store_y(g, par):
                sp.wait_ge(s_y_out, g + 1)
                hold(sp)
                sp.dma_start(out_t[:, bass.ds(g * T, T)], y_sb[par][:]).then_inc(s_stored[par], 16)

            def route(g, first):
                sp.wait_ge(S["comb_t"], g + 1)
                sp.dma_start(c_dram, comb_t[:]).then_inc(s_comb_st, 16)
                sp.wait_ge(s_comb_st, 16 * g + 16)
                hold(sp)
                for c in range(NCHUNK - 1):
                    spread(g, c, first)

            def spread(g, c, first):
                if not first:
                    sp.wait_ge(s_silu_c, E * (g - 1) + CHUNK * (c + 1))
                sp.dma_start(comb_b[:, c * CHUNK:(c + 1) * CHUNK, :],
                             c_dram[c * CHUNK:(c + 1) * CHUNK, :].rearrange("(o e) t -> o e t", o=1)
                             .to_broadcast([P, CHUNK, T])).then_inc(s_comb_b[c], 16)

            def prepare(s):
                if s == 0:
                    load_x(0, 0)
                    sp.dma_start(att_raw[:, 0, :], w1).then_inc(s_attw_in, 16)
                    for n, w in enumerate((w2, qw, kw, vw)):
                        sp.dma_start(att_raw[:, n + 1, :], w).then_inc(s_attw_in, 16)
                    sp.wait_ge(s_pad, 1)
                    sp.dma_start(att_raw[:, 5, 0:E], gate_w).then_inc(s_attw_in, 16)
                    for n, b in enumerate((b1, b2, qb, kb, vb)):
                        sp.dma_start(bias[:, n:n + 1], b).then_inc(s_small_in, 16)
                    for a in range(TILES):
                        sp.dma_start(ebias[:, a, :], expert_bias.to_broadcast([P, E]))\
                            .then_inc(s_small_in, 16)
                    for i, (lo, hi) in enumerate(EXPW):
                        sp.dma_start(exp_raw[:, lo:hi, :], wexp[:, lo:hi, :]).then_inc(s_expw_in[i], 16)
                    load_res(0, 0)
                    load_res(1, 1)

            def expert(g, par, s, first):
                if s == 0:
                    if not last_group(g):
                        load_x(g + 1, 1 - par)
                    spread(g, NCHUNK - 1, first)
                if s == 2 and not first:
                    store_y(g - 1, 1 - par)
                    if not last_group(g):
                        load_res(g + 1, 1 - par)

            def stage(g, par, s, first):
                if s == 14:
                    route(g, first)

            def finish():
                store_y(GROUPS - 1, (GROUPS - 1) % 2)
                sp.wait_ge(s_stored[0], 16 * GROUPS // 2)
                sp.wait_ge(s_stored[1], 16 * GROUPS // 2)
                sp.wait_ge(s_comb_st, 16 * GROUPS)

            program(sp, prepare, expert, stage, finish)

        @block.tensor
        def _(pe):
            mm = nc.tensor.matmul

            def project(dst, w, parts):
                for n, (a, b) in enumerate(PAIRS3):
                    last = mm(dst[:], att_w[a][:, w, :], parts[b][:], start=n == 0, stop=n == 2)
                return last

            def down(g, par, s, n_before):
                i = (par + s) % 2
                pe.wait_ge(s_h_lo, n_before + 1)
                for n, (a, b) in enumerate(PAIRS3):
                    last = mm(ps_y[:], exp_w[a][:, s, 2 * P:3 * P], h_t[i][b][:],
                              start=s == 0 and n == 0, stop=s == STEPS - 1 and n == 2,
                              skip_group_check=True)
                last.then_inc(s_down, 1)

            def attend(seq):
                for kb_ in range(2):
                    col = seq * SEQ + kb_ * (P - HALF)
                    for a, b in PAIRSPV:
                        last = mm(ps_y[:, col:col + WIN], v_nat[a][:, seq * 2 + kb_, :],
                                  p_t[b][:, seq, kb_, :], start=False, stop=False,
                                  skip_group_check=True)
                return last

            def expert(g, par, s, first):
                step = g * STEPS + s
                i = (par + s) % 2
                if first:
                    pe.wait_ge(s_expw, s + 1)
                if s == 0:
                    pe.wait_ge(S["xn_lo"], g + 1)
                if not first or s >= 2:
                    pe.wait_ge(s_silu, step - 1)
                for n, (a, b) in enumerate(PAIRS3):
                    last = mm(ps_g[i][:], exp_w[a][:, s, 0:P], xn_t[par][b][:], start=n == 0, stop=n == 2)
                last.then_inc(s_g, 1)
                if not first or s >= 2:
                    pe.wait_ge(s_h, step - 1)
                for n, (a, b) in enumerate(PAIRS3):
                    last = mm(ps_u[i][:], exp_w[a][:, s, P:2 * P], xn_t[par][b][:], start=n == 0, stop=n == 2)
                last.then_inc(s_u, 1)
                if s >= 2:
                    if s == 2 and not first:
                        pe.wait_ge(s_y_out, g)
                    down(g, par, s - 2, step - 2)
                elif not first:
                    down(g - 1, 1 - par, STEPS - 2 + s, step - 2)
                if s == 3:
                    pe.wait_ge(S["p0_lo"], g + 1)
                    pe.wait_ge(S["v2"], g + 1)
                    attend(0)
                if s == 4:
                    pe.wait_ge(S["p1_lo"], g + 1)
                    attend(1).then_inc(s_pv, 1)

            def scores(g, seq):
                dst = bank[1 + seq]
                for t in range(2):
                    o = dst[:, t * WIN:(t + 1) * WIN]
                    q0 = seq * SEQ + t * P
                    k0 = seq * SEQ + t * (P - HALF)
                    mm(o, ident_b[:], mask[:, t, :], start=True, stop=False)
                    for n, (a, b) in enumerate(PAIRS6):
                        last = mm(o, q_t[a][:, q0:q0 + P], k_t[b][:, k0:k0 + WIN],
                                  start=False, stop=n == 5)
                return last

            def turn(dst, src):
                for a in range(TILES):
                    last = nc.tensor.transpose(dst[:, a * P:(a + 1) * P], src[:, a * P:(a + 1) * P], ident[:])
                return last

            def stage(g, par, s, first):
                if s == 2:
                    if first:
                        pe.wait_ge(s_const, 1)
                    pe.wait_ge(S["xn"], g + 1)
                    if not first:
                        pe.wait_ge(S["p1_lo"], g)
                    turn(bank[0], xn[:].rearrange("p a d -> p (a d)")).then_inc(S["xn_tp"], 1)
                if s == 3:
                    pe.wait_ge(S["xn_lo"], g + 1)
                    if first:
                        pe.wait_ge(s_attw, 1)
                    if not first:
                        pe.wait_ge(S["comb_t"], g)
                    project(bank[1], 0, xn_t[par]).then_inc(S["hid_mm"], 1)
                if s == 4:
                    pe.wait_ge(S["hid_lo"], g + 1)
                    if not first:
                        pe.wait_ge(S["p0_lo"], g)
                    project(bank[2], 1, hid_t).then_inc(S["m_mm"], 1)
                if s == 5:
                    pe.wait_ge(S["m_lo"], g + 1)
                    project(bank[0], 2, m_t).then_inc(S["q_mm"], 1)
                if s == 6:
                    project(bank[1], 3, m_t).then_inc(S["k_mm"], 1)
                if s == 7:
                    project(bank[2], 4, m_t).then_inc(S["vt_mm"], 1)
                if s == 8:
                    pe.wait_ge(S["vt"], g + 1)
                    pe.wait_ge(S["q_rest"], g + 1)
                    turn(bank[0], v_t).then_inc(S["v_tp"], 1)
                if s == 9:
                    pe.wait_ge(S["q2"], g + 1)
                    pe.wait_ge(S["k2"], g + 1)
                    scores(g, 0).then_inc(S["sc0_mm"], 1)
                if s == 10:
                    scores(g, 1).then_inc(S["sc1_mm"], 1)
                    pe.wait_ge(S["v_rest"], g + 1)
                    project(bank[0], 5, xn_t[par]).then_inc(S["gate_mm"], 1)
                if s == 12:
                    pe.wait_ge(S["gate_e"], g + 1)
                    turn(bank[1], gate_e).then_inc(S["gate_tp"], 1)
                    pe.wait_ge(S["pn0"], g + 1)
                    pe.wait_ge(S["exp1"], g + 1)
                    turn_probs(bank[2], 0).then_inc(S["pt0_tp"], 1)
                if s == 13:
                    pe.wait_ge(S["pn1"], g + 1)
                    turn_probs(bank[0], 1).then_inc(S["pt1_tp"], 1)
                if s == 14:
                    pe.wait_ge(S["comb"], g + 1)
                    turn(bank[1], comb[:].rearrange("p a d -> p (a d)")).then_inc(S["comb_tp"], 1)

            def turn_probs(dst, seq):
                for kb_ in range(2):
                    for t in range(2):
                        c = kb_ * (SEQ - (P - HALF)) + t * P
                        last = nc.tensor.transpose(dst[:, c:c + P],
                                                   prob_n[:, 2 * seq + t, kb_ * P:(kb_ + 1) * P], ident[:])
                return last

            def finish():
                n = GROUPS * STEPS
                for s in (STEPS - 2, STEPS - 1):
                    down(GROUPS - 1, (GROUPS - 1) % 2, s, n - STEPS + s)

            program(pe, nothing, expert, stage, finish)

        @block.scalar
        def _(act):
            A = nc.scalar.activation

            def prepare(s):
                if s == 0:
                    act.wait_ge(s_attw_in, 16 * NA)
                    A(att_w[0][:], att_raw[:], ACT.Copy).then_inc(s_attw_hi, 1)
                for i, (lo, hi) in enumerate(EXPW):
                    if s == lo:
                        act.wait_ge(s_expw_in[i], 16)
                A(exp_w[0][:, s, :], exp_raw[:, s, :], ACT.Copy).then_inc(s_expw_hi, 1)

            def h_hi(step, i):
                act.wait_ge(s_h, step + 1)
                A(h_t[i][0][:], h[i][:], ACT.Copy).then_inc(s_h_hi, 1)

            def expert(g, par, s, first):
                step = g * STEPS + s
                i = (par + s) % 2
                act.wait_ge(s_g, step + 1)
                if not first or s >= 2:
                    act.wait_ge(s_h, step - 1)
                A(silu[i][:], ps_g[i][:], ACT.Silu).then_inc(s_silu, 1)
                if not first or s >= 1:
                    if not first or s >= 3:
                        act.wait_ge(s_down, step - 2)
                    h_hi(step - 1, 1 - i)

            def stage(g, par, s, first):
                if s == 2:
                    act.wait_ge(S["xn_tp"], g + 1)
                    A(xn_t[par][0][:], bank[0][:], ACT.Copy).then_inc(S["xn_hi"], 1)
                if s == 3:
                    if first:
                        act.wait_ge(s_small_in, 16 * (5 + TILES))
                    act.wait_ge(S["hid_mm"], g + 1)
                    if not first:
                        act.wait_ge(S["hid_lo"], g)
                    A(hid[:], bank[1][:], ACT.Relu, bias=bias[:, 0:1]).then_inc(S["hid"], 1)
                if s == 4:
                    act.wait_ge(S["m_mm"], g + 1)
                    if not first:
                        act.wait_ge(S["vt_mm"], g)
                    A(m_t[0][:], bank[2][:], ACT.Identity, bias=bias[:, 1:2]).then_inc(S["m_hi"], 1)
                if s == 5:
                    act.wait_ge(S["q_mm"], g + 1)
                    if not first:
                        act.wait_ge(S["sc1_mm"], g)
                    A(q_t[0][:], bank[0][:], ACT.Identity, bias=bias[:, 2:3]).then_inc(S["q0"], 1)
                if s == 6:
                    act.wait_ge(S["k_mm"], g + 1)
                    A(k_t[0][:], bank[1][:], ACT.Identity, bias=bias[:, 3:4]).then_inc(S["k0"], 1)
                if s == 7:
                    act.wait_ge(S["vt_mm"], g + 1)
                    if not first:
                        act.wait_ge(S["v_tp"], g)
                    A(v_t[:], bank[2][:], ACT.Copy).then_inc(S["vt"], 1)
                if s == 8:
                    act.wait_ge(S["v_tp"], g + 1)
                    if not first:
                        act.wait_ge(s_pv, g)
                    A(v_nat[0][:].rearrange("p a d -> p (a d)"), bank[0][:], ACT.Copy).then_inc(S["v0"], 1)
                if s == 11:
                    for seq in range(NB):
                        act.wait_ge(S[f"ebias{seq}"], g + 1)
                        if not first:
                            act.wait_ge(S[f"pn{seq}"], g)
                        for t in range(2):
                            n = 2 * seq + t
                            last = A(prob[:, n, t * (P - HALF):t * (P - HALF) + WIN],
                                     bank[1 + seq][:, t * WIN:(t + 1) * WIN], ACT.Exp,
                                     bias=exp_bias[:, n:n + 1], scale=SCALE,
                                     accum_out=row_sum[:, n:n + 1])
                        last.then_inc(S[f"exp{seq}"], 1)
                    act.wait_ge(S["gate_mm"], g + 1)
                    if not first:
                        act.wait_ge(S["gate_tp"], g)
                    A(gate_e[:], bank[0][:], ACT.Exp, scale=-1.0).then_inc(S["gate_e"], 1)
                if s in (12, 13):
                    seq = s - 12
                    act.wait_ge(S[f"pt{seq}_tp"], g + 1)
                    if not first and seq == 0:
                        act.wait_ge(s_pv, g)
                    A(p_t[0][:, seq, :, :], in_band(bank[2 - 2 * seq]), ACT.Copy).then_inc(S[f"p{seq}_hi"], 1)
                if s == 14:
                    act.wait_ge(S["comb_tp"], g + 1)
                    if not first:
                        act.wait_ge(s_comb_st, 16 * g)
                    A(comb_t[:], bank[1][0:E, :], ACT.Copy).then_inc(S["comb_t"], 1)

            def finish():
                n = GROUPS * STEPS
                act.wait_ge(s_down, n - 2)
                h_hi(n - 1, (GROUPS - 1 + STEPS - 1) % 2)

            program(act, prepare, expert, stage, finish)

        @block.vector
        def _(dve):
            V = nc.vector

            def prepare(s):
                if s == 0:
                    V.memset(att_raw[:, 5, :], 0.0).then_inc(s_pad, 1)
                    V.memset(prob_n[:], 0.0)
                    V.memset(comb[:], 0.0).then_inc(s_dve_const, 1)
                    dve.wait_ge(s_attw_hi, 1)
                    V.tensor_tensor(att_w[1][:], att_raw[:], att_w[0][:].bitcast(F32), ALU.subtract)\
                        .then_inc(s_attw, 1)
                dve.wait_ge(s_expw_hi, s + 1)
                V.tensor_tensor(exp_w[1][:, s, :], exp_raw[:, s, :], exp_w[0][:, s, :].bitcast(F32),
                                ALU.subtract).then_inc(s_expw, 1)

            def h_lo(step, i):
                dve.wait_ge(s_h_hi, step + 1)
                V.tensor_tensor(h_t[i][1][:], h[i][:], h_t[i][0][:].bitcast(F32), ALU.subtract)\
                    .then_inc(s_h_lo, 1)

            def expert(g, par, s, first):
                step = g * STEPS + s
                i = (par + s) % 2
                if not first or s >= 1:
                    h_lo(step - 1, 1 - i)
                dve.wait_ge(s_u, step + 1)
                if s == 0:
                    dve.wait_ge(s_silu, step + 1)
                else:
                    dve.wait_ge(s_silu_c, g * E + s)
                src = silu[i] if s == 0 else silu_c[i]
                if not first or s >= 2:
                    dve.wait_ge(s_h_lo, step - 1)
                V.tensor_tensor(h[i][:], src[:], ps_u[i][:], ALU.mult).then_inc(s_h, 1)
                if s == 1 and not first:
                    finish_group(g - 1, 1 - par)

            def finish_group(g, par):
                dve.wait_ge(s_down, (g + 1) * STEPS)
                res_count = 8 * (g + (2 - par))
                dve.wait_ge(s_xres[par], res_count)
                if not early(g):
                    dve.wait_ge(s_stored[par], res_count - 16)
                V.scalar_tensor_tensor(out=y_sb[par][:], in0=ps_y[:], scalar=bias[:, 4:5], in1=xres[par][:],
                                       op0=ALU.add, op1=ALU.add).then_inc(s_y_out, 1)

            def split(dst, src, hi, b):
                if b is None:
                    return V.tensor_tensor(dst, src, hi, ALU.subtract)
                return V.scalar_tensor_tensor(out=dst, in0=src, scalar=bias[:, b:b + 1], in1=hi,
                                              op0=ALU.add, op1=ALU.subtract)

            def stage(g, par, s, first):
                if s == 0:
                    dve.wait_ge(s_xin[par], 8 * (g + (2 - par)))
                    for a in range(TILES):
                        last = V.bn_stats(stats[:, a, :], xin[par][:, a, :])
                    last.then_inc(S["bn"], 1)
                    dve.wait_ge(S["bn"], g + 1)
                    hold(dve)
                    for a in range(TILES):
                        last = V.bn_aggr(mv[:, a, :], stats[:, a, :])
                    last.then_inc(S["aggr"], 1)
                    dve.wait_ge(S["aggr"], g + 1)
                    V.tensor_scalar(var_eps[:], mv[:, :, 1], EPS, None, ALU.add).then_inc(S["var_eps"], 1)
                if s == 1:
                    dve.wait_ge(S["rstd"], g + 1)
                    for a in range(TILES):
                        last = V.tensor_scalar(xn[:, a, :], xin[par][:, a, :], mv[:, a, 0:1],
                                               rstd[:, a:a + 1], ALU.subtract, ALU.mult)
                    last.then_inc(S["xn"], 1)
                if s == 2:
                    dve.wait_ge(S["xn_hi"], g + 1)
                    split(xn_t[par][1][:], bank[0][:], xn_t[par][0][:].bitcast(F32), None)\
                        .then_inc(S["xn_lo"], 1)
                if s == 3:
                    dve.wait_ge(S["hid"], g + 1)
                    if not first:
                        dve.wait_ge(S["m_mm"], g)
                    V.tensor_copy(hid_t[0][:], hid[:]).then_inc(S["hid_hi"], 1)
                    dve.wait_ge(S["hid_hi"], g + 1)
                    V.tensor_tensor(hid_t[1][:], hid[:], hid_t[0][:].bitcast(F32), ALU.subtract)\
                        .then_inc(S["hid_lo"], 1)
                if s == 4:
                    dve.wait_ge(S["m_hi"], g + 1)
                    split(m_t[1][:], bank[2][:], m_t[0][:].bitcast(F32), 1).then_inc(S["m_lo"], 1)
                if s == 5:
                    dve.wait_ge(S["q0"], g + 1)
                    if not first:
                        dve.wait_ge(S["q2"], g)
                    split(q_rest[:], bank[0][:], q_t[0][:], 2).then_inc(S["q_rest"], 1)
                if s == 6:
                    dve.wait_ge(S["k0"], g + 1)
                    if not first:
                        dve.wait_ge(S["k2"], g)
                    split(k_rest[:], bank[1][:], k_t[0][:], 3).then_inc(S["k_rest"], 1)
                if s == 8:
                    dve.wait_ge(S["v0"], g + 1)
                    if not first:
                        dve.wait_ge(S["v2"], g)
                    split(v_rest[:], bank[0][:], v_nat[0][:].rearrange("p a d -> p (a d)"), None)\
                        .then_inc(S["v_rest"], 1)
                if s in (9, 10):
                    seq = s - 9
                    n = slice(2 * seq, 2 * seq + 2)
                    dve.wait_ge(S[f"sc{seq}_mm"], g + 1)
                    V.tensor_reduce(neg_max[:, n], bank[1 + seq][:, 0:2 * WIN].rearrange("p (t c) -> p t c", t=2),
                                    AX.X, ALU.max, negate=True).then_inc(S[f"nmax{seq}"], 1)
                    dve.wait_ge(S[f"nmax{seq}"], g + 1)
                    V.tensor_scalar(exp_bias[:, n], neg_max[:, n], SCALE, None, ALU.mult)\
                        .then_inc(S[f"ebias{seq}"], 1)
                if s == 11:
                    if first:
                        dve.wait_ge(s_dve_const, 1)
                    for seq in range(NB):
                        n = slice(2 * seq, 2 * seq + 2)
                        dve.wait_ge(S[f"exp{seq}"], g + 1)
                        V.reciprocal(row_inv[:, n], row_sum[:, n]).then_inc(S[f"inv{seq}"], 1)
                        dve.wait_ge(S[f"inv{seq}"], g + 1)
                        for t in range(2):
                            c = t * (P - HALF)
                            last = V.tensor_scalar(prob_n[:, 2 * seq + t, c:c + WIN],
                                                   prob[:, 2 * seq + t, c:c + WIN],
                                                   row_inv[:, 2 * seq + t:2 * seq + t + 1], None, ALU.mult)
                        last.then_inc(S[f"pn{seq}"], 1)
                if s in (12, 13):
                    seq = s - 12
                    dve.wait_ge(S[f"p{seq}_hi"], g + 1)
                    V.tensor_tensor(p_t[1][:, seq, :, :], in_band(bank[2 - 2 * seq]), p_t[0][:, seq, :, :],
                                    ALU.subtract).then_inc(S[f"p{seq}_lo"], 1)
                if s == 12:
                    dve.wait_ge(S["gate_tp"], g + 1)
                    V.tensor_scalar(gate_1[:], bank[1][:].rearrange("p (a c) -> p a c", a=TILES)[:, :, 0:E],
                                    1.0, None, ALU.add).then_inc(S["gate_1"], 1)
                    dve.wait_ge(S["gate_1"], g + 1)
                    V.reciprocal(score[:], gate_1[:]).then_inc(S["score"], 1)
                    dve.wait_ge(S["score"], g + 1)
                    V.tensor_tensor(select[:], score[:], ebias[:], ALU.add).then_inc(S["select"], 1)
                    dve.wait_ge(S["select"], g + 1)
                    hold(dve)
                    for a in range(TILES):
                        last = V.max(top8[:, a, :], select[:, a, :])
                    last.then_inc(S["top8"], 1)
                if s == 13:
                    dve.wait_ge(S["top8"], g + 1)
                    hold(dve)
                    for a in range(TILES):
                        last = V.match_replace(out=rest[:, a, :], in_to_replace=top8[:, a, :],
                                               in_values=select[:, a, :], imm_value=TAKEN)
                    last.then_inc(S["rest"], 1)
                    dve.wait_ge(S["rest"], g + 1)
                    V.tensor_tensor(chosen[:], rest[:], select[:], ALU.not_equal).then_inc(S["chosen"], 1)
                    dve.wait_ge(S["chosen"], g + 1)
                    V.tensor_tensor(weight[:], chosen[:], score[:], ALU.mult).then_inc(S["weight"], 1)
                    dve.wait_ge(S["weight"], g + 1)
                    V.tensor_reduce(wsum[:], weight[:], AX.X, ALU.add).then_inc(S["wsum"], 1)
                    dve.wait_ge(S["wsum"], g + 1)
                    V.reciprocal(winv[:], wsum[:]).then_inc(S["winv"], 1)
                    dve.wait_ge(S["winv"], g + 1)
                    if not first:
                        dve.wait_ge(S["comb_tp"], g)
                    V.scalar_tensor_tensor(out=comb[:, :, 0:E], in0=weight[:], scalar=ROUTE_SCALE,
                                           in1=winv[:].rearrange("p (a o) -> p a o", o=1)
                                           .to_broadcast([P, TILES, E]),
                                           op0=ALU.mult, op1=ALU.mult).then_inc(S["comb"], 1)

            def finish():
                n = GROUPS * STEPS
                h_lo(n - 1, (GROUPS - 1 + STEPS - 1) % 2)
                finish_group(GROUPS - 1, (GROUPS - 1) % 2)

            program(dve, prepare, expert, stage, finish)

        @block.gpsimd
        def _(pool):
            G = nc.gpsimd

            def prepare(s):
                if s == 0:
                    G.memset(power[:], -0.5)
                    G.memset(ident[:], 0.0)
                    G.memset(ident_b[:], 0.0)
                    G.memset(mask[:], 0.0).then_inc(s_const0, 1)
                    pool.wait_ge(s_const0, 1)
                    for m in (ident, ident_b):
                        G.affine_select(out=m[:], in_=m[:], compare_op=ALU.not_equal, fill=1.0, base=0,
                                        pattern=[[-1, P]], channel_multiplier=1)
                    for t in range(2):
                        last = G.affine_select(out=mask[:, t, :], in_=mask[:, t, :], compare_op=ALU.is_ge,
                                               fill=MASKED, base=HALF * (1 - t), pattern=[[1, WIN]],
                                               channel_multiplier=-1)
                    last.then_inc(s_const1, 1)
                    pool.wait_ge(s_const1, 1)
                    for t in range(2):
                        last = G.affine_select(out=mask[:, t, :], in_=mask[:, t, :], compare_op=ALU.is_ge,
                                               fill=MASKED, base=HALF * (1 + t), pattern=[[-1, WIN]],
                                               channel_multiplier=1)
                    last.then_inc(s_const, 1)

            def expert(g, par, s, first):
                if s == 0:
                    return
                step = g * STEPS + s
                i = (par + s) % 2
                if (s - 1) % CHUNK == 0:
                    pool.wait_ge(s_comb_b[(s - 1) // CHUNK], 16 * g + 16)
                pool.wait_ge(s_silu, step + 1)
                G.tensor_tensor(silu_c[i][:], silu[i][:], comb_b[:, s - 1, :], ALU.mult).then_inc(s_silu_c, 1)

            def thirds(name, src, mid, low, g, first):
                pool.wait_ge(S[f"{name}_rest"], g + 1)
                hold(pool)
                G.tensor_copy(mid, src).then_inc(S[f"{name}1"], 1)
                pool.wait_ge(S[f"{name}1"], g + 1)
                G.tensor_tensor(low, src, mid, ALU.subtract).then_inc(S[f"{name}2"], 1)

            def stage(g, par, s, first):
                if s == 0:
                    pool.wait_ge(S["var_eps"], g + 1)
                    G.tensor_tensor(rstd[:], var_eps[:], power[:], ALU.pow).then_inc(S["rstd"], 1)
                if s == 5:
                    thirds("q", q_rest[:], q_t[1][:], q_t[2][:], g, first)
                if s == 6:
                    thirds("k", k_rest[:], k_t[1][:], k_t[2][:], g, first)
                if s == 8:
                    thirds("v", v_rest[:], v_nat[1][:].rearrange("p a d -> p (a d)"),
                           v_nat[2][:].rearrange("p a d -> p (a d)"), g, first)

            program(pool, prepare, expert, stage, nothing)


EXPW = [(0, 2), (2, 7), (7, 12), (12, STEPS)]


def kernel(**inputs):
    import numpy as np
    import concourse.bacc as bacc
    from concourse.bass_utils import run_bass_kernel_spmd

    a = {k: np.asarray(v) for k, v in inputs.items()}
    x = a["L0_attn_x"].reshape(SEQS * SEQ, P)
    col = lambda n: np.ascontiguousarray(a[n].reshape(-1, 1))
    gate = np.concatenate([a["L0_ffn_shared_gate_w"][None], a["L0_ffn_w_gate"]]).transpose(2, 0, 1)
    up = np.concatenate([a["L0_ffn_shared_up_w"][None], a["L0_ffn_w_up"]]).transpose(2, 0, 1)
    down = np.concatenate([a["L0_ffn_shared_down_w"][None], a["L0_ffn_w_down"]]).transpose(2, 0, 1)
    arrays = {
        "x": np.ascontiguousarray(x), "x_t": np.ascontiguousarray(x.T),
        "w1": a["L0_attn_nm_w1"], "b1": col("L0_attn_nm_b1"),
        "w2": a["L0_attn_nm_w2"], "b2": col("L0_attn_nm_b2"),
        "qw": a["L0_attn_q_w"], "qb": col("L0_attn_q_b"),
        "kw": a["L0_attn_k_w"], "kb": col("L0_attn_k_b"),
        "vw": a["L0_attn_v_w"], "vb": col("L0_attn_v_b"),
        "gate_w": np.ascontiguousarray(a["L0_ffn_gate_w"].T),
        "expert_bias": np.ascontiguousarray(a["L0_ffn_expert_bias"].reshape(1, E)),
        "wexp": np.ascontiguousarray(np.concatenate([gate, up, down], axis=2)),
    }
    nc = bacc.Bacc("TRN2", target_bir_lowering=False, num_devices=1)
    args = [nc.dram_tensor(n, v.shape, F32, kind="ExternalInput").ap() for n, v in arrays.items()]
    out_t = nc.dram_tensor("out_t", (P, SEQS * SEQ), F32, kind="ExternalOutput").ap()
    c_dram = nc.dram_tensor("c_dram", (E, T), F32, kind="Internal").ap()
    layer(nc, *args, out_t, c_dram)
    r = run_bass_kernel_spmd(nc, [arrays], core_ids=[0])
    return np.ascontiguousarray(r.results[0]["out_t"].T).reshape(SEQS, SEQ, P)
```
